# Optimizing a Trainium2 kernel written in Bass

```python
import numpy as np
import jax
import jax.numpy as jnp

def _softmax(x, axis=-1):
    return jax.nn.softmax(x, axis=axis)

def _gelu(x):
    return jax.nn.gelu(x, approximate=True)

def _silu(x):
    return jax.nn.silu(x)

def _sigmoid(x):
    return jax.nn.sigmoid(x)

def _layernorm(x, axis=-1, eps=1e-05):
    m = jnp.mean(x, axis=axis, keepdims=True)
    v = jnp.var(x, axis=axis, keepdims=True)
    return (x - m) / jnp.sqrt(v + eps)

def _scatter_add(tgt, idx, src, axis=0):
    return tgt.at[idx].add(src)

def _segment_sum(src, seg, n):
    return jax.ops.segment_sum(src, seg, n)
kernel_name = 'mk_dlrm_tower_d1_rec_r8_82cdd1'

def setup_inputs(seed: int=0):
    np.random.seed(seed)
    _w = jnp.asarray

    def _rec_inputs():
        import jax
        import jax.numpy as jnp
        _tk = jax.random.key(seed)
        ids = jnp.stack([jax.random.randint(jax.random.fold_in(_tk, 200 + f), (2048,), 0, v, jnp.int32) for f, v in enumerate([1250, 1250, 1250, 12500, 1250, 12500, 1000, 125000, 12500, 12500, 12500, 1000, 1000, 1250, 1000, 1000, 12500, 1000, 12500, 12500, 1250, 1000, 1250, 1250, 1000, 1000])], axis=1)
        tbl_0 = 0.05 * jax.random.normal(jax.random.fold_in(_tk, 500 + 0), (1250, 128), jnp.float32)
        tbl_1 = 0.05 * jax.random.normal(jax.random.fold_in(_tk, 500 + 1), (1250, 128), jnp.float32)
        tbl_2 = 0.05 * jax.random.normal(jax.random.fold_in(_tk, 500 + 2), (1250, 128), jnp.float32)
        tbl_3 = 0.05 * jax.random.normal(jax.random.fold_in(_tk, 500 + 3), (12500, 128), jnp.float32)
        tbl_4 = 0.05 * jax.random.normal(jax.random.fold_in(_tk, 500 + 4), (1250, 128), jnp.float32)
        tbl_5 = 0.05 * jax.random.normal(jax.random.fold_in(_tk, 500 + 5), (12500, 128), jnp.float32)
        tbl_6 = 0.05 * jax.random.normal(jax.random.fold_in(_tk, 500 + 6), (1000, 128), jnp.float32)
        tbl_7 = 0.05 * jax.random.normal(jax.random.fold_in(_tk, 500 + 7), (125000, 128), jnp.float32)
        tbl_8 = 0.05 * jax.random.normal(jax.random.fold_in(_tk, 500 + 8), (12500, 128), jnp.float32)
        tbl_9 = 0.05 * jax.random.normal(jax.random.fold_in(_tk, 500 + 9), (12500, 128), jnp.float32)
        tbl_10 = 0.05 * jax.random.normal(jax.random.fold_in(_tk, 500 + 10), (12500, 128), jnp.float32)
        tbl_11 = 0.05 * jax.random.normal(jax.random.fold_in(_tk, 500 + 11), (1000, 128), jnp.float32)
        tbl_12 = 0.05 * jax.random.normal(jax.random.fold_in(_tk, 500 + 12), (1000, 128), jnp.float32)
        tbl_13 = 0.05 * jax.random.normal(jax.random.fold_in(_tk, 500 + 13), (1250, 128), jnp.float32)
        tbl_14 = 0.05 * jax.random.normal(jax.random.fold_in(_tk, 500 + 14), (1000, 128), jnp.float32)
        tbl_15 = 0.05 * jax.random.normal(jax.random.fold_in(_tk, 500 + 15), (1000, 128), jnp.float32)
        tbl_16 = 0.05 * jax.random.normal(jax.random.fold_in(_tk, 500 + 16), (12500, 128), jnp.float32)
        tbl_17 = 0.05 * jax.random.normal(jax.random.fold_in(_tk, 500 + 17), (1000, 128), jnp.float32)
        tbl_18 = 0.05 * jax.random.normal(jax.random.fold_in(_tk, 500 + 18), (12500, 128), jnp.float32)
        tbl_19 = 0.05 * jax.random.normal(jax.random.fold_in(_tk, 500 + 19), (12500, 128), jnp.float32)
        tbl_20 = 0.05 * jax.random.normal(jax.random.fold_in(_tk, 500 + 20), (1250, 128), jnp.float32)
        tbl_21 = 0.05 * jax.random.normal(jax.random.fold_in(_tk, 500 + 21), (1000, 128), jnp.float32)
        tbl_22 = 0.05 * jax.random.normal(jax.random.fold_in(_tk, 500 + 22), (1250, 128), jnp.float32)
        tbl_23 = 0.05 * jax.random.normal(jax.random.fold_in(_tk, 500 + 23), (1250, 128), jnp.float32)
        tbl_24 = 0.05 * jax.random.normal(jax.random.fold_in(_tk, 500 + 24), (1000, 128), jnp.float32)
        tbl_25 = 0.05 * jax.random.normal(jax.random.fold_in(_tk, 500 + 25), (1000, 128), jnp.float32)
        _rk = jax.random.fold_in(_tk, 7)
        r_dense_x = -0.000514642 + 1.00011 * jax.random.normal(jax.random.fold_in(_rk, 101), (2048, 128), jnp.float32)
        W_top1 = 0.0456912 * jax.random.normal(jax.random.fold_in(_tk, 801), (479, 512), jnp.float32)
        W_top2 = 0.0441942 * jax.random.normal(jax.random.fold_in(_tk, 802), (512, 256), jnp.float32)
        W_top3 = 0.0625 * jax.random.normal(jax.random.fold_in(_tk, 803), (256, 1), jnp.float32)
        b_top1 = jnp.zeros((512,), jnp.float32)
        b_top2 = jnp.zeros((256,), jnp.float32)
        return (r_dense_x, ids, tbl_0, tbl_1, tbl_2, tbl_3, tbl_4, tbl_5, tbl_6, tbl_7, tbl_8, tbl_9, tbl_10, tbl_11, tbl_12, tbl_13, tbl_14, tbl_15, tbl_16, tbl_17, tbl_18, tbl_19, tbl_20, tbl_21, tbl_22, tbl_23, tbl_24, tbl_25, W_top1, b_top1, W_top2, b_top2, W_top3)
    r_dense_x, ids, tbl_0, tbl_1, tbl_2, tbl_3, tbl_4, tbl_5, tbl_6, tbl_7, tbl_8, tbl_9, tbl_10, tbl_11, tbl_12, tbl_13, tbl_14, tbl_15, tbl_16, tbl_17, tbl_18, tbl_19, tbl_20, tbl_21, tbl_22, tbl_23, tbl_24, tbl_25, W_top1, b_top1, W_top2, b_top2, W_top3 = _rec_inputs()

    def _L0_rec_setup():
        import jax, jax.numpy as jnp
        import numpy as np
        F = 26
        D = 128
        B = 2048
        _TRIU_I, _TRIU_J = np.triu_indices(F + 1, k=1)
        _TRIU_I = jnp.asarray(_TRIU_I)
        _TRIU_J = jnp.asarray(_TRIU_J)
        key = jax.random.key(seed)
        k1, k2 = jax.random.split(key)
        sparse_x = jax.random.normal(k1, (B, F, D), dtype=jnp.float32)
        dense_x = jax.random.normal(k2, (B, D), dtype=jnp.float32)
        return {'sparse_x': sparse_x, 'dense_x': dense_x}
    _L0_rec_all = _L0_rec_setup()
    _L0_rec_in = {k: v for k, v in _L0_rec_all.items() if k in ()}
    del _L0_rec_all
    return {'r_dense_x': r_dense_x, 'ids': ids, 'tbl_0': tbl_0, 'tbl_1': tbl_1, 'tbl_2': tbl_2, 'tbl_3': tbl_3, 'tbl_4': tbl_4, 'tbl_5': tbl_5, 'tbl_6': tbl_6, 'tbl_7': tbl_7, 'tbl_8': tbl_8, 'tbl_9': tbl_9, 'tbl_10': tbl_10, 'tbl_11': tbl_11, 'tbl_12': tbl_12, 'tbl_13': tbl_13, 'tbl_14': tbl_14, 'tbl_15': tbl_15, 'tbl_16': tbl_16, 'tbl_17': tbl_17, 'tbl_18': tbl_18, 'tbl_19': tbl_19, 'tbl_20': tbl_20, 'tbl_21': tbl_21, 'tbl_22': tbl_22, 'tbl_23': tbl_23, 'tbl_24': tbl_24, 'tbl_25': tbl_25, 'W_top1': W_top1, 'b_top1': b_top1, 'W_top2': W_top2, 'b_top2': b_top2, 'W_top3': W_top3}

def reference(r_dense_x, ids, tbl_0, tbl_1, tbl_2, tbl_3, tbl_4, tbl_5, tbl_6, tbl_7, tbl_8, tbl_9, tbl_10, tbl_11, tbl_12, tbl_13, tbl_14, tbl_15, tbl_16, tbl_17, tbl_18, tbl_19, tbl_20, tbl_21, tbl_22, tbl_23, tbl_24, tbl_25, W_top1, b_top1, W_top2, b_top2, W_top3):
    import jax
    import jax.numpy as jnp

    def _L0_rec_ref(sparse_x, dense_x):
        import jax, jax.numpy as jnp
        import numpy as np
        F = 26
        D = 128
        B = 2048
        _TRIU_I, _TRIU_J = np.triu_indices(F + 1, k=1)
        _TRIU_I = jnp.asarray(_TRIU_I)
        _TRIU_J = jnp.asarray(_TRIU_J)
        combined = jnp.concatenate([sparse_x, dense_x[:, None, :]], axis=1)
        interact = jnp.einsum('bfd,bgd->bfg', combined, combined)
        return interact[:, _TRIU_I, _TRIU_J]
    e = jnp.stack([tbl_0[ids[:, 0]], tbl_1[ids[:, 1]], tbl_2[ids[:, 2]], tbl_3[ids[:, 3]], tbl_4[ids[:, 4]], tbl_5[ids[:, 5]], tbl_6[ids[:, 6]], tbl_7[ids[:, 7]], tbl_8[ids[:, 8]], tbl_9[ids[:, 9]], tbl_10[ids[:, 10]], tbl_11[ids[:, 11]], tbl_12[ids[:, 12]], tbl_13[ids[:, 13]], tbl_14[ids[:, 14]], tbl_15[ids[:, 15]], tbl_16[ids[:, 16]], tbl_17[ids[:, 17]], tbl_18[ids[:, 18]], tbl_19[ids[:, 19]], tbl_20[ids[:, 20]], tbl_21[ids[:, 21]], tbl_22[ids[:, 22]], tbl_23[ids[:, 23]], tbl_24[ids[:, 24]], tbl_25[ids[:, 25]]], axis=1)
    z = _L0_rec_ref(e, r_dense_x)
    z = z.reshape(z.shape[0], -1)
    h = jnp.concatenate([z, r_dense_x], axis=1)
    h = jnp.maximum(h @ W_top1 + b_top1, 0.0)
    h = jnp.maximum(h @ W_top2 + b_top2, 0.0)
    y = h @ W_top3
    return y

_drawn_inputs = setup_inputs


def setup_inputs(seed=0):
    import zlib

    import numpy as np

    out = dict(_drawn_inputs(seed))
    spreads = {'b_top1': (0.0, 0.1), 'b_top2': (0.0, 0.1)}
    factors = {}
    for name, (base, spread) in spreads.items():
        noise = np.random.default_rng([zlib.crc32(name.encode()), seed]).standard_normal(out[name].shape)
        drawn = base * np.exp(spread * noise) if base else spread * noise
        out[name] = jnp.asarray(drawn.astype(out[name].dtype))
    for name, factor in factors.items():
        out[name] = (out[name] * factor).astype(out[name].dtype)
    return out
```

```python
from contextlib import ExitStack

import concourse.bass as bass
import numpy as np
from concourse import mybir

B, D, F = 2048, 128, 27
SIZES = [1250, 1250, 1250, 12500, 1250, 12500, 1000, 125000, 12500, 12500, 12500, 1000, 1000,
         1250, 1000, 1000, 12500, 1000, 12500, 12500, 1250, 1000, 1250, 1250, 1000, 1000]
P = 128
NB, TL, Q, G = 8, 2, 4, 32
C = B // NB
ROWS, CH = 125, 8
NT = 8
RESIDENT = [f for f in range(26) if SIZES[f] == ROWS * CH][:NT]
GATHERED = [f for f in range(26) if f not in RESIDENT]
NG = len(GATHERED)
ORDER = RESIDENT + GATHERED + [26]
FP = 32
H1, H2 = 512, 256
PAIRS = F * (F - 1) // 2
ZI, ZD = 9, 13
ZROWS = ZI * ZD
ZC = PAIRS // ZROWS


def pair_rows():
    flat = [28 * i + d for i in range(F - 1) for d in range(1, ZD + 1)]
    flat += [28 * i + 14 for i in range(PAIRS - len(flat))]
    return flat


def w1_order():
    def row(a, b):
        a, b = min(a, b), max(a, b)
        return a * (F - 1) - a * (a - 1) // 2 + b - a - 1
    rows = [row(ORDER[r // F], ORDER[r % F]) for r in pair_rows()]
    return np.array(rows + list(range(PAIRS, PAIRS + D)))


def build(nc, dense, ids, tables, w1, b1, w2, b2, w3, y):
    fp32, f32r, fp16, i32 = mybir.dt.float32, mybir.dt.float32r, mybir.dt.float16, mybir.dt.int32
    ALU, ACT = mybir.AluOpType, mybir.ActivationFunctionType

    scratch = nc.dram_tensor("scratch", (F * F, C), fp32, kind="Internal").ap()
    ids_v = ids.rearrange("(b q t g) f -> b t g q f", b=NB, q=Q, t=TL)
    dense_v = dense.rearrange("(b q t g) d -> b t g q d", b=NB, q=Q, t=TL)

    with ExitStack() as ctx:
        def sb(name, shape, dt=fp32):
            return ctx.enter_context(nc.sbuf_tensor(name, shape, dt))

        def ps(name, shape, dt=fp32):
            return ctx.enter_context(nc.psum_tensor(name, shape, dt))

        def sem(name):
            return ctx.enter_context(nc.semaphore(name))

        ident = sb("ident", [P, P])
        ident16 = sb("ident16", [P, P], fp16)
        rowid = sb("rowid", [P, CH])
        ids_all = sb("ids_all", [P, NB, TL, 26], i32)
        idx = sb("idx", [P, TL, 26], i32)
        ids16 = sb("ids16", [P, TL, NT], fp16)
        idb = sb("idb", [P, 2, 2, C], fp16)
        stage = sb("stage", [P, 2, CH * D])
        tab_hi = sb("tab_hi", [P, NT, CH, D], f32r)
        tab_lo = sb("tab_lo", [P, NT, CH, D], f32r)
        onehot = sb("onehot", [P, CH, C], f32r)
        rows = sb("rows", [P, TL, NG + 1, D])
        et = sb("et", [P, TL, P, FP])
        zc = sb("zc", [P, F, TL * G])
        z = sb("z", [P, ZC, C])
        dense_t = sb("dense_t", [P, C])
        w1s = sb("w1s", [P, ZC + 1, H1])
        w2s = sb("w2s", [P, H1 // P, H2])
        w3s = sb("w3s", [P, H2 // P])
        b1s = sb("b1s", [P, H1 // P])
        b2s = sb("b2s", [P, H2 // P])
        h1 = sb("h1", [P, H1 // P, C])
        h2 = sb("h2", [P, H2 // P, C])
        ys = sb("ys", [1, B])

        ring_t = [ps(f"ring_t{i}", [P, 512]) for i in range(2)]
        ring_m = [ps(f"ring_m{i}", [P, 512]) for i in range(2)]
        ring_g = [ps(f"ring_g{i}", [P, 8, P]) for i in range(2)]

        def feature(t, slot, n=1):
            return et[:, t, :, slot:slot + n].rearrange("d s f -> d f s")

        consts_ready = sem("consts_ready")
        memset_done = sem("memset_done")
        idents_ready = sem("idents_ready")
        ids_loaded = sem("ids_loaded")
        idx_loaded = [sem(f"idx_loaded{t}") for t in range(TL)]
        dense_loaded = [sem(f"dense_loaded{t}") for t in range(TL)]
        gathered = [sem(f"gathered{t}") for t in range(TL)]
        table_loaded = [sem(f"table_loaded{i}") for i in range(2)]
        tiles_begun = sem("tiles_begun")
        weights_loaded = sem("weights_loaded")
        hi_ready = sem("hi_ready")
        lo_ready = sem("lo_ready")
        ids16_ready = sem("ids16_ready")
        onehot_ready = sem("onehot_ready")
        onehot_used = sem("onehot_used")
        t_full, t_free = sem("t_full"), sem("t_free")
        m_full, m_free = sem("m_full"), sem("m_free")
        g_full, g_act, g_dve = sem("g_full"), sem("g_act"), sem("g_dve")
        dense_t_ready = sem("dense_t_ready")
        scratch_written = sem("scratch_written")
        z_loaded = sem("z_loaded")
        y_stored = sem("y_stored")

        PAIR = NT // 2
        TU = (NG + 1 + 3) // 4
        NTU = PAIR + TL * TU
        GU = G // 8
        MU = 4
        ZDMA = 4

        def t_use(b, k):
            return b * NTU + k

        def transposed(b, t):
            return t_use(b, PAIR + (t + 1) * TU)

        def m_use(b, k):
            return k if isinstance(b, int) and b == 0 else b * (PAIR + MU) - MU + k

        def mlp_use(b, k):
            last = isinstance(b, int) and b == NB - 1
            return m_use(b + 1, k if last else PAIR + k)

        def mlp_full(b, k):
            return b * MU + k + 1

        def g_use(b, t, u):
            return b * (TL * GU) + t * GU + u

        def early(n, depth):
            return isinstance(n, int) and n < depth

        block = ctx.enter_context(nc.Block())

        @block.sync
        def _(sp):
            def load_idx(b, t):
                sp.dma_start(idx[:, t, :], ids_v[b, t]).then_inc(idx_loaded[t], 16)

            def load_dense(b, t):
                sp.dma_start(rows[:, t, NG, :], dense_v[b, t]).then_inc(dense_loaded[t], 16)

            for t in range(TL):
                load_idx(0, t)
            with sp.Fori(0, NB) as b:
                for t in range(TL):
                    sp.dma_start(ids_all[:, b, t, :], ids_v[b, t]).then_inc(ids_loaded, 16)
            for t in range(TL):
                load_dense(0, t)
            for j, f in enumerate(RESIDENT):
                if j >= 2:
                    sp.wait_ge(hi_ready, j - 1)
                    sp.wait_ge(lo_ready, j - 1)
                src = tables[f].rearrange("(p c) d -> p (c d)", c=CH)
                sp.dma_start(stage[0:112, j % 2, :], src[0:112]).then_inc(table_loaded[j % 2], 16)
                sp.dma_start(stage[112:ROWS, j % 2, :], src[112:ROWS]).then_inc(table_loaded[j % 2], 16)
            sp.dma_start(w1s[0:ZROWS, 0:ZC, :], w1[0:PAIRS].rearrange("(k p) n -> p k n", p=ZROWS)).then_inc(weights_loaded, 16)
            sp.dma_start(w1s[:, ZC, :], w1[PAIRS:PAIRS + D]).then_inc(weights_loaded, 16)
            sp.dma_start(w2s[:, :, :], w2.rearrange("(k p) n -> p k n", p=P)).then_inc(weights_loaded, 16)
            sp.dma_start(w3s[:, :], w3).then_inc(weights_loaded, 16)
            sp.dma_start(b1s[:, :], b1).then_inc(weights_loaded, 16)
            sp.dma_start(b2s[:, :], b2).then_inc(weights_loaded, 16)

            def exchange(b):
                sp.wait_ge(g_act, (b + 1) * TL * GU)
                sp.wait_ge(g_dve, (b + 1) * TL * GU)
                if not early(b, 1):
                    sp.wait_ge(z_loaded, b * ZDMA * 16)
                for q in range(Q):
                    sp.dma_start(scratch.rearrange("(i j) c -> i j c", j=F)[:, :, q * TL * G:(q + 1) * TL * G],
                                 zc[32 * q:32 * q + F, :, :]).then_inc(scratch_written, 16)
                sp.wait_ge(scratch_written, (b + 1) * Q * 16)
                if not early(b, 1):
                    sp.wait_ge(m_full, mlp_full(b - 1, 1))
                base = scratch[0:1, :].offset
                for k in range(ZC):
                    n = min(ZI, F - 1 - ZI * k)
                    src = bass.AP(scratch.tensor, base + (28 * ZI * k + 1) * C, [[28 * C, n], [C, ZD], [1, C]])
                    sp.dma_start(z[0:n * ZD, k, :], src).then_inc(z_loaded, 16)
                src = bass.AP(scratch.tensor, base + 14 * C, [[28 * C, ZD], [1, C]])
                sp.dma_start(z[ZROWS - ZD:ZROWS, ZC - 1, :], src).then_inc(z_loaded, 16)

            def one_block(b):
                for t in range(TL):
                    sp.wait_ge(gathered[t], (b + 1) * NG * 16)
                    load_idx(b + 1, t)
                for t in range(TL):
                    sp.wait_ge(t_full, transposed(b, t))
                    load_dense(b + 1, t)
                exchange(b)

            one_block(0)
            with sp.Fori(1, NB - 1) as b:
                one_block(b)
            exchange(NB - 1)
            sp.wait_ge(m_free, mlp_use(NB - 1, MU - 1) + 1)
            sp.dma_start(y.rearrange("s o -> o s"), ys[:, :]).then_inc(y_stored, 16)
            sp.wait_ge(y_stored, 16)

        @block.gpsimd
        def _(pool):
            pool.memset(ident[:, :], 0.0).then_inc(memset_done, 1)
            pool.iota(rowid[:, :], pattern=[[1, CH]], base=0, channel_multiplier=CH,
                      allow_small_or_imprecise_dtypes=True).then_inc(consts_ready, 1)
            pool.wait_ge(memset_done, 1)
            pool.affine_select(out=ident[:, :], in_=ident[:, :], compare_op=ALU.not_equal, fill=1.0,
                               base=0, pattern=[[-1, P]], channel_multiplier=1).then_inc(consts_ready, 1)

            def gather(b, t):
                pool.wait_ge(idx_loaded[t], (b + 1) * 16)
                if not early(b, 1):
                    pool.wait_ge(t_full, transposed(b - 1, t))
                pool.sem_inc(tiles_begun, 1)
                for k, f in enumerate(GATHERED):
                    pool.indirect_dma_start(
                        out=rows[:, t, k, :], out_offset=None, in_=tables[f],
                        in_offset=bass.IndirectOffsetOnAxis(ap=idx[:, t, NT + k:NT + k + 1], axis=0),
                    ).then_inc(gathered[t], 16)

            for t in range(TL):
                gather(0, t)
            with pool.Fori(1, NB) as b:
                for t in range(TL):
                    gather(b, t)

        @block.tensor
        def _(pe):
            def t_bank(n, k):
                if not early(n, 2):
                    pe.wait_ge(t_free, n - 1)
                return ring_t[k % 2]

            def m_bank(n, k):
                if not early(n, 2):
                    pe.wait_ge(m_free, n - 1)
                return ring_m[k % 2]

            def spread_ids(b, jj):
                bank = t_bank(t_use(b, jj), jj)
                for h in range(2):
                    for t in range(TL):
                        col = (h * TL + t) * P
                        last = nc.tensor.matmul(bank[:, col:col + P],
                                                ids16[:, t, 2 * jj + h:2 * jj + h + 1].to_broadcast([P, P]),
                                                ident16[:, :], start=True, stop=True)
                last.then_inc(t_full, 1)

            def pick_rows(b, jj):
                bank = m_bank(m_use(b, jj), jj)
                for h in range(2):
                    j = 2 * jj + h
                    if early(b, 1):
                        pe.wait_ge(hi_ready, j + 1)
                        pe.wait_ge(lo_ready, j + 1)
                    out = bank[:, h * C:(h + 1) * C]
                    for c in range(CH):
                        pe.wait_ge(onehot_ready, (b * NT + j) * CH + c + 1)
                        nc.tensor.matmul(out, tab_hi[0:ROWS, j, c, :], onehot[0:ROWS, c, :],
                                         start=(c == 0), stop=False)
                        last = nc.tensor.matmul(out, tab_lo[0:ROWS, j, c, :], onehot[0:ROWS, c, :],
                                                start=False, stop=(c == CH - 1))
                        last.then_inc(onehot_used, 1)

            def one_hots(b):
                pe.wait_ge(ids16_ready, b + 1)
                spread_ids(b, 0)
                for jj in range(PAIR):
                    if jj + 1 < PAIR:
                        spread_ids(b, jj + 1)
                    pick_rows(b, jj)

            def tile(b, t):
                pe.wait_ge(gathered[t], (b + 1) * NG * 16)
                pe.wait_ge(dense_loaded[t], (b + 1) * 16)
                for u in range(TU):
                    k = PAIR + t * TU + u
                    bank = t_bank(t_use(b, k), k)
                    for f in range(4 * u, min(4 * u + 4, NG + 1)):
                        last = nc.tensor.transpose(bank[:, (f % 4) * P:(f % 4 + 1) * P], rows[:, t, f, :], ident[:, :])
                    last.then_inc(t_full, 1)

            def products(b, t):
                pe.wait_ge(t_free, transposed(b, t))
                if t == 0:
                    pe.wait_ge(m_free, m_use(b, PAIR))
                for u in range(GU):
                    n = g_use(b, t, u)
                    if not early(n, 2):
                        pe.wait_ge(g_act, n - 1)
                        pe.wait_ge(g_dve, n - 1)
                    for k in range(8):
                        four = et[:, t, (8 * u + k) * Q:(8 * u + k + 1) * Q, :]
                        last = nc.tensor.matmul(ring_g[u % 2][:, k, 0:Q * F], four.rearrange("d s f -> d (s f)"),
                                                four[:, :, 0:F], start=True, stop=True)
                    last.then_inc(g_full, 1)

            def mlp(b):
                pe.wait_ge(z_loaded, (b + 1) * ZDMA * 16)
                pe.wait_ge(dense_t_ready, (b + 1) * TL)
                for k in range(2):
                    bank = m_bank(mlp_use(b, k), k)
                    for o in (2 * k, 2 * k + 1):
                        out, cols = bank[:, (o % 2) * C:(o % 2 + 1) * C], slice(o * P, (o + 1) * P)
                        for i in range(ZC):
                            nc.tensor.matmul(out, w1s[0:ZROWS, i, cols], z[0:ZROWS, i, :], start=(i == 0), stop=False)
                        last = nc.tensor.matmul(out, w1s[:, ZC, cols], dense_t[:, :], start=False, stop=True)
                    last.then_inc(m_full, 1)
                bank = m_bank(mlp_use(b, 2), 2)
                pe.wait_ge(m_free, mlp_use(b, 2))
                for o in range(H2 // P):
                    for i in range(H1 // P):
                        last = nc.tensor.matmul(bank[:, o * C:(o + 1) * C], w2s[:, i, o * P:(o + 1) * P], h1[:, i, :],
                                                start=(i == 0), stop=(i == H1 // P - 1))
                last.then_inc(m_full, 1)
                pe.wait_ge(m_free, mlp_use(b, 3))
                for i in range(H2 // P):
                    last = nc.tensor.matmul(ring_m[1][0:1, 0:C], w3s[:, i:i + 1], h2[:, i, :],
                                            start=(i == 0), stop=(i == H2 // P - 1))
                last.then_inc(m_full, 1)

            def tiles(b):
                tile(b, 0)
                tile(b, 1)
                products(b, 0)
                products(b, 1)

            pe.wait_ge(idents_ready, 2)
            pe.wait_ge(consts_ready, 2)
            one_hots(0)
            tiles(0)
            pe.wait_ge(weights_loaded, 6 * 16)
            with pe.Fori(1, NB) as b:
                one_hots(b)
                mlp(b - 1)
                tiles(b)
            mlp(NB - 1)

        @block.scalar
        def _(act):
            def copy_ids(b, jj):
                act.wait_ge(t_full, t_use(b, jj) + 1)
                n = b * PAIR + jj
                if not early(n, 2):
                    act.wait_ge(onehot_ready, (n - 1) * 2 * CH)
                nc.scalar.copy(idb[:, jj % 2, :, :].rearrange("p h c -> p (h c)"), ring_t[jj % 2][:, :]).then_inc(t_free, 1)

            def copy_picked(b, jj):
                act.wait_ge(onehot_used, (b * NT + 2 * jj + 2) * CH)
                src = ring_m[jj % 2][:, :].rearrange("d (h t s) -> d h t s", h=2, t=TL)
                for t in range(TL):
                    last = nc.scalar.copy(feature(t, 2 * jj, 2), src[:, :, t, :])
                last.then_inc(m_free, 1)

            def copy_transposed(b, t):
                for u in range(TU):
                    k = PAIR + t * TU + u
                    act.wait_ge(t_full, t_use(b, k) + 1)
                    nf = min(4, NG + 1 - 4 * u)
                    nc.scalar.copy(feature(t, NT + 4 * u, nf),
                                   ring_t[k % 2][:, 0:nf * P].rearrange("d (f s) -> d f s", f=nf)).then_inc(t_free, 1)

            def copy_products(b, t):
                if t == 0 and not early(b, 1):
                    act.wait_ge(scratch_written, b * Q * 16)
                for u in range(GU):
                    act.wait_ge(g_full, g_use(b, t, u) + 1)
                    for q in (0, 1):
                        last = nc.scalar.copy(
                            zc[32 * q:32 * q + F, :, t * G + 8 * u:t * G + 8 * u + 8].rearrange("i j s -> i s j"),
                            ring_g[u % 2][32 * q:32 * q + F, :, F * q:F * (q + 1)])
                    last.then_inc(g_act, 1)

            def mlp(b):
                for k in range(2):
                    act.wait_ge(m_full, mlp_full(b, k))
                    for o in (2 * k, 2 * k + 1):
                        last = nc.scalar.activation(h1[:, o, :], ring_m[k % 2][:, (o % 2) * C:(o % 2 + 1) * C], ACT.Relu,
                                                    bias=b1s[:, o:o + 1])
                    last.then_inc(m_free, 1)
                act.wait_ge(m_full, mlp_full(b, 2))
                for o in range(H2 // P):
                    last = nc.scalar.activation(h2[:, o, :], ring_m[0][:, o * C:(o + 1) * C], ACT.Relu, bias=b2s[:, o:o + 1])
                last.then_inc(m_free, 1)
                act.wait_ge(m_full, mlp_full(b, 3))
                nc.scalar.copy(ys[0:1, bass.ds(b * C, C)], ring_m[1][0:1, 0:C]).then_inc(m_free, 1)

            def one_hots(b):
                copy_ids(b, 0)
                for jj in range(PAIR):
                    if jj + 1 < PAIR:
                        copy_ids(b, jj + 1)
                    copy_picked(b, jj)

            def tiles(b):
                for t in range(TL):
                    copy_transposed(b, t)
                for t in range(TL):
                    copy_products(b, t)

            for j in range(NT):
                act.wait_ge(table_loaded[j % 2], 32 * (j // 2 + 1))
                nc.scalar.copy(tab_hi[0:ROWS, j, :, :].rearrange("p c d -> p (c d)"), stage[0:ROWS, j % 2, :]).then_inc(hi_ready, 1)
            one_hots(0)
            tiles(0)
            act.wait_ge(weights_loaded, 6 * 16)
            with act.Fori(1, NB) as b:
                one_hots(b)
                mlp(b - 1)
                tiles(b)
            mlp(NB - 1)

        @block.vector
        def _(dve):
            def cast_ids(b):
                if not early(b, 1):
                    dve.wait_ge(t_full, t_use(b - 1, PAIR))
                nc.vector.tensor_copy(ids16[:, :, :], ids_all[:, b, :, 0:NT]).then_inc(ids16_ready, 1)

            def compare(b):
                for j in range(NT):
                    if j % 2 == 0:
                        dve.wait_ge(t_free, t_use(b, j // 2) + 1)
                    for c in range(CH):
                        n = (b * NT + j) * CH + c
                        if not early(n, CH):
                            dve.wait_ge(onehot_used, n - CH + 1)
                        nc.vector.tensor_scalar(onehot[0:ROWS, c, :], idb[0:ROWS, (j // 2) % 2, j % 2, :],
                                                     rowid[0:ROWS, c:c + 1], None, ALU.is_equal).then_inc(onehot_ready, 1)

            def copy_dense(b, t):
                dve.wait_ge(t_free, transposed(b, t))
                if t == 0 and not early(b, 1):
                    dve.wait_ge(m_full, mlp_full(b - 1, 1))
                nc.vector.tensor_copy(dense_t[:, :].rearrange("d (q t g) -> d q t g", q=Q, t=TL)[:, :, t, :],
                                      et[:, t, :, F - 1].rearrange("d (g q) -> d q g", q=Q)).then_inc(dense_t_ready, 1)

            def copy_products(b, t):
                if t == 0 and not early(b, 1):
                    dve.wait_ge(scratch_written, b * Q * 16)
                for u in range(GU):
                    dve.wait_ge(g_full, g_use(b, t, u) + 1)
                    for q in (2, 3):
                        last = nc.vector.tensor_copy(
                            zc[32 * q:32 * q + F, :, t * G + 8 * u:t * G + 8 * u + 8].rearrange("i j s -> i s j"),
                            ring_g[u % 2][32 * q:32 * q + F, :, F * q:F * (q + 1)])
                    last.then_inc(g_dve, 1)

            def one_block(b):
                cast_ids(b)
                compare(b)
                for t in range(TL):
                    copy_dense(b, t)
                for t in range(TL):
                    copy_products(b, t)

            nc.vector.memset(et[:, :, :, F:FP], 0.0).then_inc(idents_ready, 1)
            dve.wait_ge(consts_ready, 2)
            nc.vector.tensor_copy(ident16[:, :], ident[:, :]).then_inc(idents_ready, 1)
            for j in range(NT):
                dve.wait_ge(hi_ready, j + 1)
                nc.vector.tensor_tensor(tab_lo[0:ROWS, j, :, :].rearrange("p c d -> p (c d)"), stage[0:ROWS, j % 2, :],
                                        tab_hi[0:ROWS, j, :, :].rearrange("p c d -> p (c d)").bitcast(fp32),
                                        ALU.subtract).then_inc(lo_ready, 1)
            dve.wait_ge(ids_loaded, NB * TL * 16)
            one_block(0)
            with dve.Fori(1, NB) as b:
                one_block(b)


def kernel(**inputs):
    import concourse.bacc as _bacc
    from concourse.bass_utils import run_bass_kernel_spmd as _run

    nc = _bacc.Bacc("TRN2", target_bir_lowering=False, num_devices=1)
    arrays, args = {}, {}

    def give(name, a):
        a = np.ascontiguousarray(a)
        arrays[f"in_{name}"] = a
        args[name] = nc.dram_tensor(f"in_{name}", a.shape, mybir.dt.from_np(a.dtype), kind="ExternalInput").ap()
        return args[name]

    tables = [give(f"tbl_{f}", inputs[f"tbl_{f}"]) for f in range(26)]
    dense = give("r_dense_x", inputs["r_dense_x"])
    ids = give("ids", np.asarray(inputs["ids"])[:, ORDER[:26]])
    w1 = give("W_top1", np.asarray(inputs["W_top1"])[w1_order()])
    w2 = give("W_top2", inputs["W_top2"])
    b1, b2, w3 = (give(n, np.asarray(inputs[n]).reshape(-1, P).T) for n in ("b_top1", "b_top2", "W_top3"))
    y = nc.dram_tensor("out_y", (B, 1), mybir.dt.float32, kind="ExternalOutput").ap()
    build(nc, dense, ids, tables, w1, b1, w2, b2, w3, y)
    r = _run(nc, [arrays], core_ids=[0])
    return r.results[0]["out_y"]
```

```python
from contextlib import ExitStack

import concourse.bass as bass
import numpy as np
from concourse import mybir

B, D, F = 2048, 128, 27
SIZES = [1250, 1250, 1250, 12500, 1250, 12500, 1000, 125000, 12500, 12500, 12500, 1000, 1000,
         1250, 1000, 1000, 12500, 1000, 12500, 12500, 1250, 1000, 1250, 1250, 1000, 1000]
P = 128
NB, TL, Q, G = 8, 2, 4, 32
C = B // NB
ROWS, CH = 125, 8
NT = 8
RESIDENT = [f for f in range(26) if SIZES[f] == ROWS * CH][:NT]
GATHERED = [f for f in range(26) if f not in RESIDENT]
NG = len(GATHERED)
ORDER = RESIDENT + GATHERED + [26]
FP = 32
H1, H2 = 512, 256
PAIRS = F * (F - 1) // 2
ZI, ZD = 9, 13
ZROWS = ZI * ZD
ZC = PAIRS // ZROWS


def pair_rows():
    flat = [28 * i + d for i in range(F - 1) for d in range(1, ZD + 1)]
    flat += [28 * i + 14 for i in range(PAIRS - len(flat))]
    return flat


def w1_order():
    def row(a, b):
        a, b = min(a, b), max(a, b)
        return a * (F - 1) - a * (a - 1) // 2 + b - a - 1
    rows = [row(ORDER[r // F], ORDER[r % F]) for r in pair_rows()]
    return np.array(rows + list(range(PAIRS, PAIRS + D)))


def build(nc, dense, row_ids, col_ids, tables, w1, b1, w2, b2, w3, y):
    fp32, f32r, i32 = mybir.dt.float32, mybir.dt.float32r, mybir.dt.int32
    ALU, ACT = mybir.AluOpType, mybir.ActivationFunctionType

    scratch = nc.dram_tensor("scratch", (F * F, C), fp32, kind="Internal").ap()
    row_ids_v = row_ids.rearrange("(b q t g) f -> b t g q f", b=NB, q=Q, t=TL)
    dense_v = dense.rearrange("(b q t g) d -> b t g q d", b=NB, q=Q, t=TL)

    with ExitStack() as ctx:
        def sb(name, shape, dt=fp32):
            return ctx.enter_context(nc.sbuf_tensor(name, shape, dt))

        def ps(name, shape, dt=fp32):
            return ctx.enter_context(nc.psum_tensor(name, shape, dt))

        def sem(name):
            return ctx.enter_context(nc.semaphore(name))

        ident = sb("ident", [P, P])
        rowid = sb("rowid", [P, CH])
        ids_all = sb("ids_all", [P, NB, TL, NG], i32)
        idx = sb("idx", [P, TL, NG], i32)
        idb = sb("idb", [P, NT, C], i32)
        stage = sb("stage", [P, 2, CH * D])
        tab_hi = sb("tab_hi", [P, NT, CH, D], f32r)
        tab_lo = sb("tab_lo", [P, NT, CH, D], f32r)
        onehot = sb("onehot", [P, CH, C], f32r)
        rows = sb("rows", [P, TL, NG + 1, D])
        et = sb("et", [P, TL, P, FP])
        zc = sb("zc", [P, F, TL * G])
        z = sb("z", [P, ZC, C])
        dense_t = sb("dense_t", [P, C])
        w1s = sb("w1s", [P, ZC + 1, H1])
        w2s = sb("w2s", [P, H1 // P, H2])
        w3s = sb("w3s", [P, H2 // P])
        b1s = sb("b1s", [P, H1 // P])
        b2s = sb("b2s", [P, H2 // P])
        h1 = sb("h1", [P, H1 // P, C])
        h2 = sb("h2", [P, H2 // P, C])
        ys = sb("ys", [1, B])

        ring_t = [ps(f"ring_t{i}", [P, 512]) for i in range(2)]
        ring_m = [ps(f"ring_m{i}", [P, 512]) for i in range(2)]
        ring_g = [ps(f"ring_g{i}", [P, 8, P]) for i in range(2)]
        l1_bank = [ring_g[1][:, 4 * k:4 * k + 4, :].rearrange("p a c -> p (a c)") for k in range(2)]
        l2_bank, l3_bank = ring_m[1][:, :], ring_m[0][0:1, :]

        def feature(t, slot, n=1):
            return et[:, t, :, slot:slot + n].rearrange("d s f -> d f s")

        memset_done = sem("memset_done")
        consts_ready = sem("consts_ready")
        pad_ready = sem("pad_ready")
        ids0_loaded = sem("ids0_loaded")
        ids_loaded = sem("ids_loaded")
        idx_ready = sem("idx_ready")
        idb_loaded = sem("idb_loaded")
        dense_loaded = [sem(f"dense_loaded{t}") for t in range(TL)]
        gathered = [sem(f"gathered{t}") for t in range(TL)]
        table_loaded = [sem(f"table_loaded{i}") for i in range(2)]
        tiles_begun = sem("tiles_begun")
        weights_loaded = sem("weights_loaded")
        hi_ready = sem("hi_ready")
        lo_ready = sem("lo_ready")
        onehot_ready = sem("onehot_ready")
        onehot_used = sem("onehot_used")
        picked_copied = sem("picked_copied")
        t_full, t_free = sem("t_full"), sem("t_free")
        g_full, g_act, g_dve = sem("g_full"), sem("g_act"), sem("g_dve")
        dense_t_ready = sem("dense_t_ready")
        scratch_written = sem("scratch_written")
        z_loaded = sem("z_loaded")
        l1_full, h1_ready = sem("l1_full"), sem("h1_ready")
        l2_full, h2_ready = sem("l2_full"), sem("h2_ready")
        l3_full, y_ready = sem("l3_full"), sem("y_ready")
        y_stored = sem("y_stored")

        PAIR = NT // 2
        TU = (NG + 1 + 3) // 4
        GU = G // 8
        ZDMA = 4
        STEPS = NT
        T_STEP = 2
        L1_STEP = 4

        def transposed(b, t):
            return (b * TL + t + 1) * TU

        def picked_before_mlp_ends(b):
            return NB * PAIR if isinstance(b, int) and b == NB - 1 else (b + 2) * PAIR

        def g_use(b, t, u):
            return b * (TL * GU) + t * GU + u

        def early(n, depth):
            return isinstance(n, int) and n < depth

        def turns(j):
            every = [(t, u) for t in range(TL) for u in range(TU)]
            return every[2 * (j - T_STEP):2 * (j - T_STEP) + 2] if j >= T_STEP else []

        block = ctx.enter_context(nc.Block())

        @block.sync
        def _(sp):
            def load_dense(b, t):
                sp.dma_start(rows[:, t, NG, :], dense_v[b, t]).then_inc(dense_loaded[t], 16)

            def load_idb(b):
                sp.dma_start(idb[:, :, :], col_ids[:, bass.ds(b * C, C)].partition_broadcast(P)).then_inc(idb_loaded, 16)

            def load_table(j):
                if j >= 2:
                    sp.wait_ge(hi_ready, j - 1)
                    sp.wait_ge(lo_ready, j - 1)
                src = tables[RESIDENT[j]].rearrange("(p c) d -> p (c d)", c=CH)
                for rows_ in (slice(0, 112), slice(112, ROWS)):
                    sp.dma_start(stage[rows_, j % 2, :], src[rows_]).then_inc(table_loaded[j % 2], 16)

            for t in range(TL):
                sp.dma_start(ids_all[:, 0, t, :], row_ids_v[0, t]).then_inc(ids0_loaded, 16)
            load_table(0)
            load_idb(0)
            for j in range(1, NT):
                load_table(j)
            for t in range(TL):
                load_dense(0, t)
            with sp.Fori(1, NB) as b:
                for t in range(TL):
                    sp.dma_start(ids_all[:, b, t, :], row_ids_v[b, t]).then_inc(ids_loaded, 16)
            sp.dma_start(w1s[0:ZROWS, 0:ZC, :], w1[0:PAIRS].rearrange("(k p) n -> p k n", p=ZROWS)).then_inc(weights_loaded, 16)
            sp.dma_start(w1s[:, ZC, :], w1[PAIRS:PAIRS + D]).then_inc(weights_loaded, 16)
            sp.dma_start(w2s[:, :, :], w2.rearrange("(k p) n -> p k n", p=P)).then_inc(weights_loaded, 16)
            sp.dma_start(w3s[:, :], w3).then_inc(weights_loaded, 16)
            sp.dma_start(b1s[:, :], b1).then_inc(weights_loaded, 16)
            sp.dma_start(b2s[:, :], b2).then_inc(weights_loaded, 16)

            def exchange(b):
                sp.wait_ge(g_act, (b + 1) * TL * GU)
                sp.wait_ge(g_dve, (b + 1) * TL * GU)
                if not early(b, 1):
                    sp.wait_ge(z_loaded, b * ZDMA * 16)
                for q in range(Q):
                    sp.dma_start(scratch.rearrange("(i j) c -> i j c", j=F)[:, :, q * TL * G:(q + 1) * TL * G],
                                 zc[32 * q:32 * q + F, :, :]).then_inc(scratch_written, 16)
                sp.wait_ge(scratch_written, (b + 1) * Q * 16)
                if not early(b, 1):
                    sp.wait_ge(l1_full, b * 2)
                base = scratch[0:1, :].offset
                for k in range(ZC):
                    n = min(ZI, F - 1 - ZI * k)
                    src = bass.AP(scratch.tensor, base + (28 * ZI * k + 1) * C, [[28 * C, n], [C, ZD], [1, C]])
                    sp.dma_start(z[0:n * ZD, k, :], src).then_inc(z_loaded, 16)
                src = bass.AP(scratch.tensor, base + 14 * C, [[28 * C, ZD], [1, C]])
                sp.dma_start(z[ZROWS - ZD:ZROWS, ZC - 1, :], src).then_inc(z_loaded, 16)

            def next_inputs(b):
                for t in range(TL):
                    sp.wait_ge(t_full, transposed(b - 1, t))
                    load_dense(b, t)
                sp.wait_ge(onehot_ready, b * NT * CH)
                load_idb(b)

            next_inputs(1)
            exchange(0)
            with sp.Fori(1, NB - 1) as b:
                next_inputs(b + 1)
                exchange(b)
            exchange(NB - 1)
            sp.wait_ge(y_ready, NB)
            sp.dma_start(y.rearrange("s o -> o s"), ys[:, :]).then_inc(y_stored, 16)
            sp.wait_ge(y_stored, 16)

        @block.gpsimd
        def _(pool):
            def gather(t, indices):
                for k, f in enumerate(GATHERED):
                    pool.indirect_dma_start(
                        out=rows[:, t, k, :], out_offset=None, in_=tables[f],
                        in_offset=bass.IndirectOffsetOnAxis(ap=indices[:, k:k + 1], axis=0),
                    ).then_inc(gathered[t], 16)

            pool.memset(ident[:, :], 0.0).then_inc(memset_done, 1)
            pool.iota(rowid[:, :], pattern=[[1, CH]], base=0, channel_multiplier=CH,
                      allow_small_or_imprecise_dtypes=True).then_inc(consts_ready, 1)
            pool.wait_ge(memset_done, 1)
            pool.affine_select(out=ident[:, :], in_=ident[:, :], compare_op=ALU.not_equal, fill=1.0,
                               base=0, pattern=[[-1, P]], channel_multiplier=1).then_inc(consts_ready, 1)
            pool.wait_ge(ids0_loaded, TL * 16)
            for t in range(TL):
                gather(t, ids_all[:, 0, t, :])
            pool.wait_ge(ids_loaded, (NB - 1) * TL * 16)
            with pool.Fori(1, NB) as b:
                for t in range(TL):
                    pool.wait_ge(gathered[t], b * NG * 16)
                    pool.wait_ge(t_full, transposed(b - 1, t))
                    pool.tensor_copy(idx[:, t, :], ids_all[:, b, t, :]).then_inc(idx_ready, 1)
                    pool.wait_ge(idx_ready, (b - 1) * TL + t + 1)
                    pool.sem_inc(tiles_begun, 1)
                    gather(t, idx[:, t, :])

        @block.tensor
        def _(pe):
            def pick_rows(b, j):
                if j % 2 == 0 and not early(b * PAIR + j // 2, 2):
                    pe.wait_ge(picked_copied, b * PAIR + j // 2 - 1)
                if j == 0 and not early(b, 2):
                    pe.wait_ge(y_ready, b - 1)
                if early(b, 1):
                    pe.wait_ge(hi_ready, j + 1)
                    pe.wait_ge(lo_ready, j + 1)
                out = ring_m[(j // 2) % 2][:, (j % 2) * C:(j % 2 + 1) * C]
                for c in range(CH):
                    pe.wait_ge(onehot_ready, (b * NT + j) * CH + c + 1)
                    nc.tensor.matmul(out, tab_hi[0:ROWS, j, c, :], onehot[0:ROWS, c, :], start=(c == 0), stop=False)
                    nc.tensor.matmul(out, tab_lo[0:ROWS, j, c, :], onehot[0:ROWS, c, :],
                                     start=False, stop=(c == CH - 1)).then_inc(onehot_used, 1)

            def transpose_rows(b, t, u):
                if u == 0:
                    pe.wait_ge(gathered[t], (b + 1) * NG * 16)
                    pe.wait_ge(dense_loaded[t], (b + 1) * 16)
                n = (b * TL + t) * TU + u
                if not early(n, 2):
                    pe.wait_ge(t_free, n - 1)
                for f in range(4 * u, min(4 * u + 4, NG + 1)):
                    last = nc.tensor.transpose(ring_t[(t * TU + u) % 2][:, (f % 4) * P:(f % 4 + 1) * P],
                                               rows[:, t, f, :], ident[:, :])
                last.then_inc(t_full, 1)

            def products(b, t):
                pe.wait_ge(t_free, transposed(b, t))
                pe.wait_ge(picked_copied, (b + 1) * PAIR)
                for u in range(GU):
                    n = g_use(b, t, u)
                    if not early(n, 2):
                        pe.wait_ge(g_act, n - 1)
                        pe.wait_ge(g_dve, n - 1)
                    if t == 0 and not early(b, 1):
                        if u == 1:
                            layer2(b - 1)
                        if u == 2:
                            layer3(b - 1)
                    for k in range(8):
                        four = et[:, t, (8 * u + k) * Q:(8 * u + k + 1) * Q, :]
                        last = nc.tensor.matmul(ring_g[u % 2][:, k, 0:Q * F], four.rearrange("d s f -> d (s f)"),
                                                four[:, :, 0:F], start=True, stop=True)
                    last.then_inc(g_full, 1)

            def layer1(b, o):
                if o == 0:
                    pe.wait_ge(z_loaded, (b + 1) * ZDMA * 16)
                    pe.wait_ge(dense_t_ready, (b + 1) * TL)
                    pe.wait_ge(g_act, (b + 1) * TL * GU)
                    pe.wait_ge(g_dve, (b + 1) * TL * GU)
                out, cols = l1_bank[o // 2][:, (o % 2) * C:(o % 2 + 1) * C], slice(o * P, (o + 1) * P)
                for i in range(ZC):
                    nc.tensor.matmul(out, w1s[0:ZROWS, i, cols], z[0:ZROWS, i, :], start=(i == 0), stop=False)
                last = nc.tensor.matmul(out, w1s[:, ZC, cols], dense_t[:, :], start=False, stop=True)
                if o % 2 == 1:
                    last.then_inc(l1_full, 1)

            def layer2(b):
                pe.wait_ge(h1_ready, (b + 1) * 2)
                pe.wait_ge(picked_copied, picked_before_mlp_ends(b))
                for o in range(H2 // P):
                    for i in range(H1 // P):
                        last = nc.tensor.matmul(l2_bank[:, o * C:(o + 1) * C], w2s[:, i, o * P:(o + 1) * P], h1[:, i, :],
                                                start=(i == 0), stop=(i == H1 // P - 1))
                last.then_inc(l2_full, 1)

            def layer3(b):
                pe.wait_ge(h2_ready, b + 1)
                for i in range(H2 // P):
                    last = nc.tensor.matmul(l3_bank[:, 0:C], w3s[:, i:i + 1], h2[:, i, :],
                                            start=(i == 0), stop=(i == H2 // P - 1))
                last.then_inc(l3_full, 1)

            pe.wait_ge(pad_ready, 1)
            pe.wait_ge(consts_ready, 2)
            for j in range(NT):
                pick_rows(0, j)
            for t in range(TL):
                for u in range(TU):
                    transpose_rows(0, t, u)
                products(0, t)
            pe.wait_ge(weights_loaded, 6 * 16)
            with pe.Fori(1, NB) as b:
                for j in range(STEPS):
                    for t, u in turns(j):
                        transpose_rows(b, t, u)
                    pick_rows(b, j)
                    if L1_STEP <= j < L1_STEP + H1 // P:
                        layer1(b - 1, j - L1_STEP)
                for t in range(TL):
                    products(b, t)
            for o in range(H1 // P):
                layer1(NB - 1, o)
            layer2(NB - 1)
            layer3(NB - 1)

        @block.scalar
        def _(act):
            def copy_picked(b, jj):
                act.wait_ge(onehot_used, (b * NT + 2 * jj + 2) * CH)
                src = ring_m[jj % 2][:, :].rearrange("d (h q t g) -> d h q t g", h=2, q=Q, t=TL)
                for t in range(TL):
                    out = et[:, t, :, 2 * jj:2 * jj + 2].rearrange("d (g q) f -> d f q g", q=Q)
                    last = nc.scalar.copy(out, src[:, :, :, t, :])
                last.then_inc(picked_copied, 1)

            def copy_transposed(b, t, u):
                act.wait_ge(t_full, (b * TL + t) * TU + u + 1)
                nf = min(4, NG + 1 - 4 * u)
                nc.scalar.copy(feature(t, NT + 4 * u, nf),
                               ring_t[(t * TU + u) % 2][:, 0:nf * P].rearrange("d (f s) -> d f s", f=nf)).then_inc(t_free, 1)

            def copy_products(b, t):
                if t == 0 and not early(b, 1):
                    act.wait_ge(scratch_written, b * Q * 16)
                for u in range(GU):
                    if t == 0 and not early(b, 1):
                        if u == 1:
                            relu2(b - 1)
                        if u == 2:
                            copy_y(b - 1)
                    act.wait_ge(g_full, g_use(b, t, u) + 1)
                    for q in (0, 1):
                        last = nc.scalar.copy(
                            zc[32 * q:32 * q + F, :, t * G + 8 * u:t * G + 8 * u + 8].rearrange("i j s -> i s j"),
                            ring_g[u % 2][32 * q:32 * q + F, :, F * q:F * (q + 1)])
                    last.then_inc(g_act, 1)

            def relu1(b, k):
                act.wait_ge(l1_full, b * 2 + k + 1)
                for o in (2 * k, 2 * k + 1):
                    last = nc.scalar.activation(h1[:, o, :], l1_bank[k][:, (o % 2) * C:(o % 2 + 1) * C], ACT.Relu,
                                                bias=b1s[:, o:o + 1])
                last.then_inc(h1_ready, 1)

            def relu2(b):
                act.wait_ge(l2_full, b + 1)
                for o in range(H2 // P):
                    last = nc.scalar.activation(h2[:, o, :], l2_bank[:, o * C:(o + 1) * C], ACT.Relu, bias=b2s[:, o:o + 1])
                last.then_inc(h2_ready, 1)

            def copy_y(b):
                act.wait_ge(l3_full, b + 1)
                nc.scalar.copy(ys[0:1, bass.ds(b * C, C)], l3_bank[:, 0:C]).then_inc(y_ready, 1)

            for j in range(NT):
                act.wait_ge(table_loaded[j % 2], 32 * (j // 2 + 1))
                nc.scalar.copy(tab_hi[0:ROWS, j, :, :].rearrange("p c d -> p (c d)"), stage[0:ROWS, j % 2, :]).then_inc(hi_ready, 1)
                if j >= 3 and j % 2 == 1:
                    copy_picked(0, j // 2 - 1)
            copy_picked(0, PAIR - 1)
            for t in range(TL):
                for u in range(TU):
                    copy_transposed(0, t, u)
                copy_products(0, t)
            act.wait_ge(weights_loaded, 6 * 16)
            with act.Fori(1, NB) as b:
                for j in range(STEPS):
                    for t, u in turns(j):
                        copy_transposed(b, t, u)
                    if j % 2 == 1:
                        copy_picked(b, j // 2)
                    if j in (L1_STEP + 1, L1_STEP + 3):
                        relu1(b - 1, (j - L1_STEP) // 2)
                for t in range(TL):
                    copy_products(b, t)
            for k in range(2):
                relu1(NB - 1, k)
            relu2(NB - 1)
            copy_y(NB - 1)

        @block.vector
        def _(dve):
            def compare(b, j, chunks=range(CH)):
                if j == 0 and chunks[0] == 0:
                    dve.wait_ge(idb_loaded, (b + 1) * 16)
                for c in chunks:
                    n = (b * NT + j) * CH + c
                    if not early(n, CH):
                        dve.wait_ge(onehot_used, n - CH + 1)
                    nc.vector.tensor_scalar(onehot[0:ROWS, c, :], idb[0:ROWS, j, :],
                                            rowid[0:ROWS, c:c + 1], None, ALU.is_equal).then_inc(onehot_ready, 1)

            def copy_dense(b, t):
                dve.wait_ge(t_free, transposed(b, t))
                if t == 0 and not early(b, 1):
                    dve.wait_ge(l1_full, b * 2)
                nc.vector.tensor_copy(dense_t[:, :].rearrange("d (q t g) -> d q t g", q=Q, t=TL)[:, :, t, :],
                                      et[:, t, :, F - 1].rearrange("d (g q) -> d q g", q=Q)).then_inc(dense_t_ready, 1)

            def copy_products(b, t, ahead=True):
                if t == 0 and not early(b, 1):
                    dve.wait_ge(scratch_written, b * Q * 16)
                for u in range(GU):
                    if t == TL - 1 and ahead:
                        compare(b + 1, 0, range(u * CH // GU, (u + 1) * CH // GU))
                    dve.wait_ge(g_full, g_use(b, t, u) + 1)
                    for q in (2, 3):
                        last = nc.vector.tensor_copy(
                            zc[32 * q:32 * q + F, :, t * G + 8 * u:t * G + 8 * u + 8].rearrange("i j s -> i s j"),
                            ring_g[u % 2][32 * q:32 * q + F, :, F * q:F * (q + 1)])
                    last.then_inc(g_dve, 1)

            nc.vector.memset(et[:, :, :, F:FP], 0.0).then_inc(pad_ready, 1)
            dve.wait_ge(consts_ready, 2)
            for j in range(NT):
                dve.wait_ge(hi_ready, j + 1)
                nc.vector.tensor_tensor(tab_lo[0:ROWS, j, :, :].rearrange("p c d -> p (c d)"), stage[0:ROWS, j % 2, :],
                                        tab_hi[0:ROWS, j, :, :].rearrange("p c d -> p (c d)").bitcast(fp32),
                                        ALU.subtract).then_inc(lo_ready, 1)
                compare(0, j)
            for t in range(TL):
                copy_dense(0, t)
                copy_products(0, t)
            def rest_of_block(b, ahead):
                for j in range(1, STEPS):
                    compare(b, j)
                for t in range(TL):
                    copy_dense(b, t)
                for t in range(TL):
                    copy_products(b, t, ahead)

            with dve.Fori(1, NB - 1) as b:
                rest_of_block(b, True)
            rest_of_block(NB - 1, False)


def kernel(**inputs):
    import concourse.bacc as _bacc
    from concourse.bass_utils import run_bass_kernel_spmd as _run

    nc = _bacc.Bacc("TRN2", target_bir_lowering=False, num_devices=1)
    arrays, args = {}, {}

    def give(name, a):
        a = np.ascontiguousarray(a)
        arrays[f"in_{name}"] = a
        args[name] = nc.dram_tensor(f"in_{name}", a.shape, mybir.dt.from_np(a.dtype), kind="ExternalInput").ap()
        return args[name]

    tables = [give(f"tbl_{f}", inputs[f"tbl_{f}"]) for f in range(26)]
    dense = give("r_dense_x", inputs["r_dense_x"])
    ids = np.asarray(inputs["ids"])
    row_ids = give("row_ids", ids[:, GATHERED])
    col_ids = give("col_ids", ids[:, RESIDENT].T)
    w1 = give("W_top1", np.asarray(inputs["W_top1"])[w1_order()])
    w2 = give("W_top2", inputs["W_top2"])
    b1, b2, w3 = (give(n, np.asarray(inputs[n]).reshape(-1, P).T) for n in ("b_top1", "b_top2", "W_top3"))
    y = nc.dram_tensor("out_y", (B, 1), mybir.dt.float32, kind="ExternalOutput").ap()
    build(nc, dense, row_ids, col_ids, tables, w1, b1, w2, b2, w3, y)
    r = _run(nc, [arrays], core_ids=[0])
    return r.results[0]["out_y"]
```

```python
from contextlib import ExitStack

import concourse.bass as bass
import numpy as np
from concourse import mybir

B, D, F = 2048, 128, 27
SIZES = [1250, 1250, 1250, 12500, 1250, 12500, 1000, 125000, 12500, 12500, 12500, 1000, 1000,
         1250, 1000, 1000, 12500, 1000, 12500, 12500, 1250, 1000, 1250, 1250, 1000, 1000]
P = 128
NB, TL, Q, G = 8, 2, 4, 32
C = B // NB
ROWS, CH = 125, 8
NT = 8
RESIDENT = [f for f in range(26) if SIZES[f] == ROWS * CH][:NT]
GATHERED = [f for f in range(26) if f not in RESIDENT]
NG = len(GATHERED)
ORDER = RESIDENT + GATHERED + [26]
FP = 32
H1, H2 = 512, 256
PAIRS = F * (F - 1) // 2
ZI, ZD = 9, 13
ZROWS = ZI * ZD
ZC = PAIRS // ZROWS


def pair_rows():
    flat = [28 * i + d for i in range(F - 1) for d in range(1, ZD + 1)]
    flat += [28 * i + 14 for i in range(PAIRS - len(flat))]
    return flat


def w1_order():
    def row(a, b):
        a, b = min(a, b), max(a, b)
        return a * (F - 1) - a * (a - 1) // 2 + b - a - 1
    rows = [row(ORDER[r // F], ORDER[r % F]) for r in pair_rows()]
    return np.array(rows + list(range(PAIRS, PAIRS + D)))


def build(nc, dense_t, row_ids, col_ids, tables, w1, b1, w2, b2, w3, y):
    fp32, f32r, i32 = mybir.dt.float32, mybir.dt.float32r, mybir.dt.int32
    ALU, ACT = mybir.AluOpType, mybir.ActivationFunctionType

    scratch = nc.dram_tensor("scratch", (F * F, C), fp32, kind="Internal").ap()

    with ExitStack() as ctx:
        def sb(name, shape, dt=fp32):
            return ctx.enter_context(nc.sbuf_tensor(name, shape, dt))

        def ps(name, shape, dt=fp32):
            return ctx.enter_context(nc.psum_tensor(name, shape, dt))

        def sem(name):
            return ctx.enter_context(nc.semaphore(name))

        ident = sb("ident", [P, P])
        ones = sb("ones", [P, 1])
        rowid = sb("rowid", [P, CH])
        ids_all = sb("ids_all", [P, NB, TL, NG], i32)
        idx = sb("idx", [P, TL, NG], i32)
        stage = sb("stage", [P, 2, CH * D])
        idb = sb("idb", [P, NT, C], i32)
        tab_hi = sb("tab_hi", [P, NT, CH, D], f32r)
        tab_lo = sb("tab_lo", [P, NT, CH, D], f32r)
        onehot = sb("onehot", [P, 2 * CH, C], f32r)
        rows = sb("rows", [P, TL, NG, D])
        dense_x = sb("dense_x", [P, C])
        et = sb("et", [P, TL, P, FP])
        zc = sb("zc", [P, F, TL * G])
        z = sb("z", [P, ZC, C])
        z_hi, z_lo = (sb(n, [P, ZC, C], f32r) for n in ("z_hi", "z_lo"))
        dense_hi, dense_lo = (sb(n, [P, C], f32r) for n in ("dense_hi", "dense_lo"))
        w1_hi, w1_lo = (sb(n, [P, ZC + 1, H1], f32r) for n in ("w1_hi", "w1_lo"))
        w2_hi, w2_lo = (sb(n, [P, H1 // P, H2], f32r) for n in ("w2_hi", "w2_lo"))
        w3s = sb("w3s", [P, H2 // P])
        b1s = sb("b1s", [P, H1 // P])
        b2s = sb("b2s", [P, H2 // P])
        h1 = sb("h1", [P, 2, C])
        h1_hi, h1_lo = (sb(n, [P, H1 // P, C], f32r) for n in ("h1_hi", "h1_lo"))
        h2 = sb("h2", [P, H2 // P, C])
        terms_hi, terms_lo = (sb(n, [P, C], f32r) for n in ("terms_hi", "terms_lo"))
        ones_r = sb("ones_r", [P, 1], f32r)
        ys = sb("ys", [1, C])

        ring_t = [ps(f"ring_t{i}", [P, 512]) for i in range(2)]
        ring_m = [ps(f"ring_m{i}", [P, 512]) for i in range(2)]
        ring_g = [ps(f"ring_g{i}", [P, 8, P]) for i in range(2)]
        l3_bank = ring_m[0][0:1, :]

        def g_bank(k):
            return ring_g[k // 2][:, 4 * (k % 2):4 * (k % 2) + 4, :].rearrange("p a c -> p (a c)")

        def last_block(b):
            return isinstance(b, int) and b == NB - 1

        L1_UNITS, L2_UNITS = H1 // P, H2 // P

        def h1_parts(b):
            return [[o] for o in range(L1_UNITS)] if at_end(b) else [[0, 1], [2, 3]]

        def at_end(b):
            return isinstance(b, int) and b >= NB - 2

        def l1_out(b, o):
            if at_end(b):
                banks = [g_bank(2), g_bank(3), *ring_t] if last_block(b) else [*ring_t, *ring_m]
                return banks[o][:, 0:C]
            return g_bank(2 + o // 2)[:, (o % 2) * C:(o % 2 + 1) * C]

        def l2_out(b, o):
            if at_end(b):
                banks = [ring_m[1], g_bank(0)] if last_block(b) else [g_bank(0), g_bank(1)]
                return banks[o][:, 0:C]
            return ring_m[1][:, o * C:(o + 1) * C]

        def feature(t, slot, n=1):
            return et[:, t, :, slot:slot + n].rearrange("d s f -> d f s")

        memset_done = sem("memset_done")
        consts_ready = sem("consts_ready")
        pad_ready = sem("pad_ready")
        ids0_loaded, ids_loaded = sem("ids0_loaded"), sem("ids_loaded")
        idx_ready = sem("idx_ready")
        idb_loaded = [sem(f"idb_loaded{i}") for i in range(2)]
        dense_loaded, dense_copied = sem("dense_loaded"), sem("dense_copied")
        table_loaded = [sem(f"table_loaded{i}") for i in range(2)]
        tiles_begun = sem("tiles_begun")
        weights_loaded = sem("weights_loaded")
        hi_ready = sem("hi_ready")
        lo_ready = sem("lo_ready")
        onehot_ready = sem("onehot_ready")
        onehot_used = sem("onehot_used")
        picked_copied = sem("picked_copied")
        rows_transposed, transposed_copied = sem("rows_transposed"), sem("transposed_copied")
        products_ready, products_copied_act, products_copied_dve = sem("products_ready"), sem("products_copied_act"), sem("products_copied_dve")
        dense_hi_ready, dense_lo_ready = sem("dense_hi_ready"), sem("dense_lo_ready")
        z_hi_ready, z_lo_ready = ([sem(f"{n}{k}") for k in range(ZC)] for n in ("z_hi_ready", "z_lo_ready"))
        h1_hi_ready, h1_lo_ready = sem("h1_hi_ready"), sem("h1_lo_ready")
        scratch_written = sem("scratch_written")
        z_loaded = [sem(f"z_loaded{k}") for k in range(ZC)]
        l1_full, h1_ready = sem("l1_full"), sem("h1_ready")
        ones_set, h2_summed, terms_hi_ready = sem("ones_set"), sem("h2_summed"), sem("terms_hi_ready")
        h2_scaled, terms_ready = sem("h2_scaled"), sem("terms_ready")
        l2_full, h2_ready = sem("l2_full"), sem("h2_ready")
        l3_full, y_ready = sem("l3_full"), sem("y_ready")
        y_stored = sem("y_stored")

        PAIR = NT // 2
        TU = (NG + 3) // 4
        TSIZE = [min(4, NG - 4 * u) for u in range(TU)]
        GROWS = (Q - 1) * FP + F
        GU = G // 8
        ZDMAS = [1, 1, 2]
        STEPS = NT
        T_STEP = 4
        WEIGHT_USES = (1, 2, TL * GU - 2)
        L1_STEP = 6

        gathered = [[sem(f"gathered{t}_{u}") for u in range(TU)] for t in range(TL)]

        def transposed(b, t):
            return (b * TL + t + 1) * TU

        def picked_before_mlp_ends(b):
            return NB * PAIR if isinstance(b, int) else (b + 2) * PAIR

        def g_use(b, t, u):
            return b * (TL * GU) + t * GU + u

        def early(n, depth):
            return isinstance(n, int) and n < depth

        def mlp_inside(b):
            return not (early(b, 1) or last_block(b))

        def onehot_slot(j, c):
            return (j % 2) * CH + c

        def turns0(j):
            return range(TU)[2 * (j - T_STEP):2 * (j - T_STEP) + 2] if j >= T_STEP else []

        def turns1(b, t, u):
            if early(b, 1):
                uses = [[0], [], [1], [2], [3, 4]]
            elif last_block(b):
                uses = [[0, 1], [2], [], [3, 4]]
            else:
                uses = [[], [0], [1, 2], [3, 4]]
            return uses[t * GU + u] if t * GU + u < len(uses) else []

        block = ctx.enter_context(nc.Block())

        @block.sync
        def _(sp):
            def load_dense(b):
                sp.dma_start(dense_x[:, :], dense_t[:, bass.ds(b * C, C)]).then_inc(dense_loaded, 16)

            def load_idb(b, part):
                tabs = slice(1, NT) if part else slice(0, 1)
                sp.dma_start(idb[:, tabs, :], col_ids[tabs, bass.ds(b * C, C)].partition_broadcast(P)).then_inc(idb_loaded[part], 16)

            def load_table(j):
                if j >= 2:
                    sp.wait_ge(hi_ready, j - 1)
                    sp.wait_ge(lo_ready, j - 1)
                src = tables[RESIDENT[j]].rearrange("(p c) d -> p (c d)", c=CH)
                for rows_ in (slice(0, 112), slice(112, ROWS)):
                    sp.dma_start(stage[rows_, j % 2, :], src[rows_]).then_inc(table_loaded[j % 2], 16)

            sp.dma_start(ids_all[:, 0, :, :], row_ids[:, 0]).then_inc(ids0_loaded, 16)
            load_idb(0, 0)
            load_table(0)
            load_table(1)
            load_idb(0, 1)
            load_dense(0)
            for j in range(2, NT):
                load_table(j)
            sp.dma_start(ids_all[:, 1:NB, :, :], row_ids[:, 1:NB]).then_inc(ids_loaded, 16)
            for k in range(ZC + 1):
                if k % 2 == 0:
                    sp.wait_ge(hi_ready, NT - 1 + k // 2)
                    sp.wait_ge(lo_ready, NT - 1 + k // 2)
                n = ZROWS if k < ZC else D
                sp.dma_start(stage[0:n, k // 2, (k % 2) * H1:(k % 2 + 1) * H1],
                             w1[k * ZROWS:k * ZROWS + n]).then_inc(table_loaded[k // 2], 16)
            sp.dma_start(w3s[:, :], w3).then_inc(weights_loaded, 16)
            sp.dma_start(b1s[:, :], b1).then_inc(weights_loaded, 16)
            sp.dma_start(b2s[:, :], b2).then_inc(weights_loaded, 16)

            def store_y(b):
                sp.wait_ge(y_ready, b + 1)
                sp.dma_start(y[bass.ds(b * C, C), :].rearrange("s o -> o s"), ys[:, :]).then_inc(y_stored, 16)

            def exchange(b):
                if not early(b, 1):
                    sp.wait_ge(z_lo_ready[ZC - 1], b)
                for t in range(TL) if last_block(b) else [TL - 1]:
                    sp.wait_ge(products_copied_act, (b * TL + t + 1) * GU)
                    sp.wait_ge(products_copied_dve, (b * TL + t + 1) * GU)
                    first, n = (t * G, G) if last_block(b) else (0, TL * G)
                    for q in range(Q):
                        c = q * TL * G + first
                        sp.dma_start(scratch.rearrange("(i j) c -> i j c", j=F)[:, :, c:c + n],
                                     zc[32 * q:32 * q + F, :, first:first + n]).then_inc(scratch_written, 16)
                sp.wait_ge(scratch_written, (b + (TL if last_block(b) else 1)) * Q * 16)
                base = scratch[0:1, :].offset
                for k in range(ZC):
                    n = min(ZI, F - 1 - ZI * k)
                    src = bass.AP(scratch.tensor, base + (28 * ZI * k + 1) * C, [[28 * C, n], [C, ZD], [1, C]])
                    sp.dma_start(z[0:n * ZD, k, :], src).then_inc(z_loaded[k], 16)
                src = bass.AP(scratch.tensor, base + 14 * C, [[28 * C, ZD], [1, C]])
                sp.dma_start(z[ZROWS - ZD:ZROWS, ZC - 1, :], src).then_inc(z_loaded[ZC - 1], 16)

            def next_inputs(b):
                sp.wait_ge(onehot_ready, b * NT * CH)
                for part in range(2):
                    load_idb(b, part)
                sp.wait_ge(dense_copied, b)
                sp.wait_ge(dense_lo_ready, b)
                load_dense(b)

            next_inputs(1)
            sp.wait_ge(hi_ready, NT + 1)
            sp.wait_ge(lo_ready, NT + 1)
            sp.dma_start(stage[:, 0, :].rearrange("p (k n) -> p k n", n=H2),
                         w2.rearrange("(k p) n -> p k n", p=P)).then_inc(table_loaded[0], 16)
            exchange(0)
            with sp.Fori(1, NB - 1) as b:
                next_inputs(b + 1)
                exchange(b)
                store_y(b - 1)
            exchange(NB - 1)
            store_y(NB - 2)
            store_y(NB - 1)
            sp.wait_ge(y_stored, NB * 16)

        @block.gpsimd
        def _(pool):
            def gather(t, indices):
                for k, f in enumerate(GATHERED):
                    pool.indirect_dma_start(
                        out=rows[:, t, k, :], out_offset=None, in_=tables[f],
                        in_offset=bass.IndirectOffsetOnAxis(ap=indices[:, k:k + 1], axis=0),
                    ).then_inc(gathered[t][k // 4], 16)

            pool.memset(ident[:, :], 0.0).then_inc(memset_done, 1)
            pool.iota(rowid[:, :], pattern=[[1, CH]], base=0, channel_multiplier=CH,
                      allow_small_or_imprecise_dtypes=True).then_inc(consts_ready, 1)
            pool.wait_ge(memset_done, 1)
            pool.affine_select(out=ident[:, :], in_=ident[:, :], compare_op=ALU.not_equal, fill=1.0,
                               base=0, pattern=[[-1, P]], channel_multiplier=1).then_inc(consts_ready, 1)
            pool.wait_ge(ids0_loaded, 16)
            for t in range(TL):
                gather(t, ids_all[:, 0, t, :])
            with pool.Fori(1, NB) as b:
                for t in range(TL):
                    pool.wait_ge(idx_ready, (b - 1) * TL + t + 1)
                    pool.sem_inc(tiles_begun, 1)
                    gather(t, idx[:, t, :])

        @block.tensor
        def _(pe):
            def pick_rows(b, j):
                if j % 2 == 0 and not early(b * PAIR + j // 2, 2):
                    pe.wait_ge(picked_copied, b * PAIR + j // 2 - 1)
                if j == 0 and not early(b, 2):
                    pe.wait_ge(y_ready, b - 1)
                if early(b, 1):
                    pe.wait_ge(hi_ready, j + 1)
                    pe.wait_ge(lo_ready, j + 1)
                out = ring_m[(j // 2) % 2][:, (j % 2) * C:(j % 2 + 1) * C]
                for c in range(CH):
                    pe.wait_ge(onehot_ready, (b * NT + j) * CH + c + 1)
                    chosen = onehot[0:ROWS, onehot_slot(j, c), :]
                    nc.tensor.matmul(out, tab_hi[0:ROWS, j, c, :], chosen, start=(c == 0), stop=False)
                    nc.tensor.matmul(out, tab_lo[0:ROWS, j, c, :], chosen,
                                     start=False, stop=(c == CH - 1)).then_inc(onehot_used, 1)

            def transpose_rows(b, t, u):
                pe.wait_ge(gathered[t][u], (b + 1) * TSIZE[u] * 16)
                n = (b * TL + t) * TU + u
                if not early(n, 2):
                    pe.wait_ge(transposed_copied, n - 1)
                for f in range(4 * u, 4 * u + TSIZE[u]):
                    last = nc.tensor.transpose(ring_t[(t * TU + u) % 2][:, (f % 4) * P:(f % 4 + 1) * P],
                                               rows[:, t, f, :], ident[:, :])
                last.then_inc(rows_transposed, 1)

            def products(b, t):
                for v in turns1(b, t, 0):
                    transpose_rows(b, 1, v)
                if t == 0:
                    pe.wait_ge(transposed_copied, transposed(b, 0))
                    pe.wait_ge(picked_copied, (b + 1) * PAIR)
                    pe.wait_ge(dense_copied, b + 1)
                for u in range(GU):
                    for v in turns1(b, t, u) if u > 0 else []:
                        transpose_rows(b, 1, v)
                    if t == 1 and u == 0:
                        pe.wait_ge(transposed_copied, transposed(b, 1))
                    n = g_use(b, t, u)
                    if not early(n, 2):
                        pe.wait_ge(products_copied_act, n - 1)
                        pe.wait_ge(products_copied_dve, n - 1)
                    if t == 0 and mlp_inside(b):
                        if u == 1:
                            pe.wait_ge(h1_ready, b * L1_UNITS)
                        if u == 2:
                            layer2(b - 1)
                    if (t, u) == (1, 0) and mlp_inside(b):
                        layer3(b - 1)
                    for k in range(8):
                        four = et[:, t, (8 * u + k) * Q:(8 * u + k + 1) * Q, :]
                        last = nc.tensor.matmul(ring_g[u % 2][0:GROWS, k, 0:Q * F],
                                                four.rearrange("d s f -> d (s f)")[:, 0:GROWS],
                                                four[:, :, 0:F], start=True, stop=True)
                    last.then_inc(products_ready, 1)

            def times(out, w_hi, w_lo, x_hi, x_lo, start, stop):
                nc.tensor.matmul(out, w_hi, x_lo, start=start, stop=False)
                nc.tensor.matmul(out, w_lo, x_hi, start=False, stop=False)
                return nc.tensor.matmul(out, w_hi, x_hi, start=False, stop=stop)

            def wait_for_layer1(b):
                pe.wait_ge(lo_ready, NT + 3)
                pe.wait_ge(dense_lo_ready, b + 1)
                if isinstance(b, int) and b == NB - 2:
                    pe.wait_ge(transposed_copied, transposed(NB - 1, TL - 1))
                else:
                    pe.wait_ge(products_copied_act, (b + 1) * TL * GU)
                    pe.wait_ge(products_copied_dve, (b + 1) * TL * GU)

            def layer1(b, o, i):
                k = (i - 1) % (ZC + 1)
                n, cols = ZROWS if k < ZC else D, slice(o * P, (o + 1) * P)
                if o == 0 and k < ZC:
                    pe.wait_ge(z_lo_ready[k], b + 1)
                x_hi, x_lo = (z_hi[0:n, k, :], z_lo[0:n, k, :]) if k < ZC else (dense_hi[:, :], dense_lo[:, :])
                last = times(l1_out(b, o), w1_hi[0:n, k, cols], w1_lo[0:n, k, cols], x_hi, x_lo, i == 0, i == ZC)
                if i == ZC:
                    last.then_inc(l1_full, 1)

            def layer2(b):
                pe.wait_ge(picked_copied, picked_before_mlp_ends(b))
                if at_end(b):
                    pe.wait_ge(products_copied_act, NB * TL * GU)
                    pe.wait_ge(products_copied_dve, NB * TL * GU)
                terms = [(o, i) for o in range(H2 // P) for i in range(H1 // P)]
                if at_end(b):
                    terms.sort(key=lambda term: term[1])
                ends = {part[0]: part[-1] for part in h1_parts(b)}
                for o, i in terms:
                    if o == 0 and i in ends:
                        pe.wait_ge(h1_lo_ready, b * L1_UNITS + ends[i] + 1)
                    cols = slice(o * P, (o + 1) * P)
                    last = times(l2_out(b, o), w2_hi[:, i, cols], w2_lo[:, i, cols],
                                 h1_hi[:, i, :], h1_lo[:, i, :], i == 0, i == H1 // P - 1)
                    if i == H1 // P - 1:
                        last.then_inc(l2_full, 1)

            def layer3(b):
                if isinstance(b, int):
                    for i in range(H2 // P):
                        pe.wait_ge(h2_ready, b * L2_UNITS + i + 1)
                        last = nc.tensor.matmul(l3_bank[:, 0:C], w3s[:, i:i + 1], h2[:, i, :],
                                                start=(i == 0), stop=(i == H2 // P - 1))
                else:
                    pe.wait_ge(terms_ready, b + 1)
                    nc.tensor.matmul(l3_bank[:, 0:C], ones_r[:, :], terms_lo[:, :], start=True, stop=False)
                    last = nc.tensor.matmul(l3_bank[:, 0:C], ones_r[:, :], terms_hi[:, :], start=False, stop=True)
                last.then_inc(l3_full, 1)

            pe.wait_ge(pad_ready, 2)
            pe.wait_ge(consts_ready, 2)
            def one_block(b):
                for j in range(STEPS):
                    for u in turns0(j):
                        transpose_rows(b, 0, u)
                    pick_rows(b, j)
                    if j >= L1_STEP and mlp_inside(b):
                        if j == L1_STEP:
                            wait_for_layer1(b - 1)
                        for o in (2 * (j - L1_STEP), 2 * (j - L1_STEP) + 1):
                            for i in range(ZC + 1):
                                layer1(b - 1, o, i)
                for t in range(TL):
                    products(b, t)

            one_block(0)
            pe.wait_ge(weights_loaded, 3 * 16)
            with pe.Fori(1, NB - 1) as b:
                one_block(b)
            one_block(NB - 1)
            wait_for_layer1(NB - 2)
            for o in range(H1 // P):
                for i in range(ZC + 1):
                    layer1(NB - 2, o, i)
            layer2(NB - 2)
            wait_for_layer1(NB - 1)
            for i in range(ZC + 1):
                for o in range(H1 // P):
                    layer1(NB - 1, o, i)
            layer3(NB - 2)
            layer2(NB - 1)
            layer3(NB - 1)

        @block.scalar
        def _(act):
            def copy_picked(b, jj):
                act.wait_ge(onehot_used, (b * NT + 2 * jj + 2) * CH)
                src = ring_m[jj % 2][:, :].rearrange("d (h q t g) -> d h q t g", h=2, q=Q, t=TL)
                for t in range(TL):
                    out = et[:, t, :, 2 * jj:2 * jj + 2].rearrange("d (g q) f -> d f q g", q=Q)
                    last = nc.scalar.copy(out, src[:, :, :, t, :])
                last.then_inc(picked_copied, 1)

            def copy_transposed(b, t, u):
                act.wait_ge(rows_transposed, (b * TL + t) * TU + u + 1)
                nf = TSIZE[u]
                nc.scalar.copy(feature(t, NT + 4 * u, nf),
                               ring_t[(t * TU + u) % 2][:, 0:nf * P].rearrange("d (f s) -> d f s", f=nf)).then_inc(transposed_copied, 1)

            def weight_hi(part):
                if part < 2:
                    act.wait_ge(table_loaded[part], 32 * (NT // 2 + 1))
                    for c in (2 * part, 2 * part + 1):
                        n = ZROWS if c < ZC else D
                        last = nc.scalar.copy(w1_hi[0:n, c, :], stage[0:n, part, (c % 2) * H1:(c % 2 + 1) * H1])
                else:
                    act.wait_ge(table_loaded[0], 32 * (NT // 2 + 1) + 16)
                    last = nc.scalar.copy(w2_hi[:, :, :].rearrange("p k n -> p (k n)"), stage[:, 0, :])
                last.then_inc(hi_ready, 1)

            def copy_products(b, t):
                if t == 0 and not early(b, 1):
                    act.wait_ge(scratch_written, b * Q * 16)
                for u in range(GU):
                    for v in turns1(b, t, u):
                        copy_transposed(b, 1, v)
                    if t == 0 and mlp_inside(b):
                        if u == 2:
                            relu2(b - 1)
                    if (t, u) == (1, 0) and mlp_inside(b):
                        copy_y(b - 1)
                    act.wait_ge(products_ready, g_use(b, t, u) + 1)
                    for q in (0, 1):
                        last = nc.scalar.copy(
                            zc[32 * q:32 * q + F, :, t * G + 8 * u:t * G + 8 * u + 8].rearrange("i j s -> i s j"),
                            ring_g[u % 2][32 * q:32 * q + F, :, F * q:F * (q + 1)])
                    last.then_inc(products_copied_act, 1)
                    if early(b, 1) and t * GU + u in WEIGHT_USES:
                        weight_hi(WEIGHT_USES.index(t * GU + u))

            def relu1(b, part):
                act.wait_ge(l1_full, b * L1_UNITS + part[-1] + 1)
                if not (part[0] == 0 and early(b, 1)):
                    act.wait_ge(h1_lo_ready, b * L1_UNITS + part[-1] + 1 - 2)
                for o in part:
                    nc.scalar.activation(h1[:, o % 2, :], l1_out(b, o), ACT.Relu, bias=b1s[:, o:o + 1]).then_inc(h1_ready, 1)

            def relu2(b):
                for o in range(L2_UNITS):
                    act.wait_ge(l2_full, b * L2_UNITS + (o + 1 if at_end(b) else L2_UNITS))
                    nc.scalar.activation(h2[:, o, :], l2_out(b, o), ACT.Relu, bias=b2s[:, o:o + 1]).then_inc(h2_ready, 1)

            def copy_y(b):
                act.wait_ge(l3_full, b + 1)
                if not early(b, 1):
                    act.wait_ge(y_stored, b * 16)
                nc.scalar.copy(ys[0:1, :], l3_bank[:, 0:C]).then_inc(y_ready, 1)

            def copy_dense(b):
                act.wait_ge(dense_loaded, (b + 1) * 16)
                if not early(b, 1):
                    act.wait_ge(products_ready, b * TL * GU)
                nc.scalar.copy(et[:, :, :, F - 1].rearrange("d t (g q) -> d q t g", q=Q),
                               dense_x[:, :].rearrange("d (q t g) -> d q t g", q=Q, t=TL)).then_inc(dense_copied, 1)

            def step(b, j):
                if j == 2:
                    copy_dense(b)
                for u in turns0(j):
                    copy_transposed(b, 0, u)
                if j == L1_STEP + 1 and mlp_inside(b):
                    relu1(b - 1, [0, 1])
                if j % 2 == 1:
                    copy_picked(b, j // 2)
                if j == L1_STEP + 1 and mlp_inside(b):
                    relu1(b - 1, [2, 3])

            for j in range(NT):
                act.wait_ge(table_loaded[j % 2], 32 * (j // 2 + 1))
                nc.scalar.copy(tab_hi[0:ROWS, j, :, :].rearrange("p c d -> p (c d)"), stage[0:ROWS, j % 2, :]).then_inc(hi_ready, 1)
                if j >= 1:
                    step(0, j - 1)
            step(0, NT - 1)
            for t in range(TL):
                copy_products(0, t)
            act.wait_ge(weights_loaded, 3 * 16)
            def rest_of_block(b):
                for j in range(STEPS):
                    step(b, j)
                for t in range(TL):
                    copy_products(b, t)

            with act.Fori(1, NB - 1) as b:
                rest_of_block(b)
            rest_of_block(NB - 1)
            for b in (NB - 2, NB - 1):
                for part in h1_parts(b):
                    relu1(b, part)
                if b == NB - 1:
                    copy_y(NB - 2)
                relu2(b)
            copy_y(NB - 1)

        @block.vector
        def _(dve):
            def compare(b, j, chunks=range(CH)):
                if j <= 1 and chunks[0] == 0:
                    dve.wait_ge(idb_loaded[j], (b + 1) * 16)
                for c in chunks:
                    n = (b * NT + j) * CH + c
                    if not early(n, 2 * CH):
                        dve.wait_ge(onehot_used, n - 2 * CH + 1)
                    nc.vector.tensor_scalar(onehot[0:ROWS, onehot_slot(j, c), :], idb[0:ROWS, j, :],
                                            rowid[0:ROWS, c:c + 1], None, ALU.is_equal).then_inc(onehot_ready, 1)

            def split_dense(b):
                dve.wait_ge(dense_loaded, (b + 1) * 16)
                if not early(b, 1):
                    dve.wait_ge(l1_full, b * L1_UNITS)
                nc.vector.tensor_copy(dense_hi[:, :], dense_x[:, :]).then_inc(dense_hi_ready, 1)
                dve.wait_ge(dense_hi_ready, b + 1)
                nc.vector.tensor_tensor(dense_lo[:, :], dense_x[:, :], dense_hi[:, :].bitcast(fp32),
                                        ALU.subtract).then_inc(dense_lo_ready, 1)

            def split_z(b):
                if not early(b, 1):
                    dve.wait_ge(l1_full, b * L1_UNITS)
                for k in range(ZC):
                    dve.wait_ge(z_loaded[k], (b + 1) * ZDMAS[k] * 16)
                    src, hi, lo = (x[0:ZROWS, k, :] for x in (z, z_hi, z_lo))
                    nc.vector.tensor_copy(hi, src).then_inc(z_hi_ready[k], 1)
                    dve.wait_ge(z_hi_ready[k], b + 1)
                    nc.vector.tensor_tensor(lo, src, hi.bitcast(fp32), ALU.subtract).then_inc(z_lo_ready[k], 1)

            def split_h1(b, part):
                dve.wait_ge(h1_ready, b * L1_UNITS + part[-1] + 1)
                if part[0] == 0 and not early(b, 1):
                    dve.wait_ge(l2_full, b * L2_UNITS)
                first, n = part[0], len(part)
                src = h1[:, first % 2:first % 2 + n, :].rearrange("p k c -> p (k c)")
                hi, lo = (x[:, first:first + n, :].rearrange("p k c -> p (k c)") for x in (h1_hi, h1_lo))
                nc.vector.tensor_copy(hi, src).then_inc(h1_hi_ready, n)
                dve.wait_ge(h1_hi_ready, b * L1_UNITS + part[-1] + 1)
                nc.vector.tensor_tensor(lo, src, hi.bitcast(fp32), ALU.subtract).then_inc(h1_lo_ready, n)

            def layer3_terms(b):
                dve.wait_ge(h2_ready, (b + 1) * L2_UNITS)
                nc.vector.tensor_scalar(h2[:, 0, :], h2[:, 0, :], w3s[:, 0:1], None, ALU.mult).then_inc(h2_scaled, 1)
                dve.wait_ge(h2_scaled, b + 1)
                nc.vector.scalar_tensor_tensor(h2[:, 0, :], h2[:, 1, :], w3s[:, 1:2], h2[:, 0, :],
                                               ALU.mult, ALU.add).then_inc(h2_summed, 1)
                dve.wait_ge(h2_summed, b + 1)
                nc.vector.tensor_copy(terms_hi[:, :], h2[:, 0, :]).then_inc(terms_hi_ready, 1)
                dve.wait_ge(terms_hi_ready, b + 1)
                nc.vector.tensor_tensor(terms_lo[:, :], h2[:, 0, :], terms_hi[:, :].bitcast(fp32),
                                        ALU.subtract).then_inc(terms_ready, 1)

            def weight_lo(part):
                dve.wait_ge(hi_ready, NT + part + 1)
                if part < 2:
                    for c in (2 * part, 2 * part + 1):
                        n = ZROWS if c < ZC else D
                        last = nc.vector.tensor_tensor(w1_lo[0:n, c, :], stage[0:n, part, (c % 2) * H1:(c % 2 + 1) * H1],
                                                       w1_hi[0:n, c, :].bitcast(fp32), ALU.subtract)
                else:
                    w2_parts = (x[:, :, :].rearrange("p k n -> p (k n)") for x in (w2_lo, w2_hi))
                    last = nc.vector.tensor_tensor(next(w2_parts), stage[:, 0, :], next(w2_parts).bitcast(fp32), ALU.subtract)
                last.then_inc(lo_ready, 1)

            def compare_ahead(b, use):
                first = GU - 2
                share = 2 * CH // (TL * GU - first) + 1
                for n in range(2 * CH)[share * (use - first):share * (use - first + 1)] if use >= first else []:
                    compare(b, n // CH, range(n % CH, n % CH + 1))

            def place_indices(b, t):
                if early(b, 2):
                    dve.wait_ge(ids_loaded, 16)
                dve.wait_ge(rows_transposed, transposed(b - 1, t))
                nc.vector.tensor_copy(idx[:, t, :], ids_all[:, b, t, :]).then_inc(idx_ready, 1)

            def copy_products(b, t, ahead=True):
                if t == 0 and not early(b, 1):
                    dve.wait_ge(scratch_written, b * Q * 16)
                if ahead and (early(b, 1) or t == 1):
                    place_indices(b + 1, t)
                for u in range(GU):
                    if ahead:
                        compare_ahead(b + 1, t * GU + u)
                    if t == 0 and u == 2 and mlp_inside(b):
                        layer3_terms(b - 1)
                    dve.wait_ge(products_ready, g_use(b, t, u) + 1)
                    for q in (2, 3):
                        last = nc.vector.tensor_copy(
                            zc[32 * q:32 * q + F, :, t * G + 8 * u:t * G + 8 * u + 8].rearrange("i j s -> i s j"),
                            ring_g[u % 2][32 * q:32 * q + F, :, F * q:F * (q + 1)])
                    last.then_inc(products_copied_dve, 1)
                    if early(b, 1) and t * GU + u in WEIGHT_USES:
                        weight_lo(WEIGHT_USES.index(t * GU + u))

            nc.vector.memset(ones[:, :], 1.0).then_inc(ones_set, 1)
            nc.vector.memset(et[:, :, :, F:FP], 0.0).then_inc(pad_ready, 1)
            dve.wait_ge(ones_set, 1)
            nc.vector.tensor_copy(ones_r[:, :], ones[:, :]).then_inc(pad_ready, 1)
            dve.wait_ge(consts_ready, 2)
            for j in range(NT):
                if j == 0:
                    compare(0, j)
                dve.wait_ge(hi_ready, j + 1)
                nc.vector.tensor_tensor(tab_lo[0:ROWS, j, :, :].rearrange("p c d -> p (c d)"), stage[0:ROWS, j % 2, :],
                                        tab_hi[0:ROWS, j, :, :].rearrange("p c d -> p (c d)").bitcast(fp32),
                                        ALU.subtract).then_inc(lo_ready, 1)
                if j >= 1:
                    compare(0, j)
            split_dense(0)
            for t in range(TL):
                copy_products(0, t)

            def rest_of_block(b, ahead):
                for j in range(2, STEPS):
                    compare(b, j)
                    if j == L1_STEP:
                        split_z(b - 1)
                if ahead:
                    place_indices(b + 1, 0)
                if mlp_inside(b):
                    split_h1(b - 1, [0, 1])
                    split_dense(b)
                    split_h1(b - 1, [2, 3])
                for t in range(TL):
                    copy_products(b, t, ahead)

            dve.wait_ge(weights_loaded, 3 * 16)
            with dve.Fori(1, NB - 1) as b:
                rest_of_block(b, True)
            rest_of_block(NB - 1, False)
            for b in (NB - 2, NB - 1):
                if b == NB - 1:
                    split_dense(b)
                    split_z(b)
                for part in h1_parts(b):
                    split_h1(b, part)


def kernel(**inputs):
    import concourse.bacc as _bacc
    from concourse.bass_utils import run_bass_kernel_spmd as _run

    nc = _bacc.Bacc("TRN2", target_bir_lowering=False, num_devices=1)
    arrays, args = {}, {}

    def give(name, a):
        a = np.ascontiguousarray(a)
        arrays[f"in_{name}"] = a
        args[name] = nc.dram_tensor(f"in_{name}", a.shape, mybir.dt.from_np(a.dtype), kind="ExternalInput").ap()
        return args[name]

    tables = [give(f"tbl_{f}", inputs[f"tbl_{f}"]) for f in range(26)]
    dense_t = give("r_dense_x", np.asarray(inputs["r_dense_x"]).T)
    ids = np.asarray(inputs["ids"])
    row_ids = give("row_ids", ids[:, GATHERED].reshape(NB, Q, TL, G, NG).transpose(3, 1, 0, 2, 4).reshape(P, NB, TL, NG))
    col_ids = give("col_ids", ids[:, RESIDENT].T)
    w1 = give("W_top1", np.asarray(inputs["W_top1"])[w1_order()])
    w2 = give("W_top2", inputs["W_top2"])
    b1, b2, w3 = (give(n, np.asarray(inputs[n]).reshape(-1, P).T) for n in ("b_top1", "b_top2", "W_top3"))
    y = nc.dram_tensor("out_y", (B, 1), mybir.dt.float32, kind="ExternalOutput").ap()
    build(nc, dense_t, row_ids, col_ids, tables, w1, b1, w2, b2, w3, y)
    r = _run(nc, [arrays], core_ids=[0])
    return r.results[0]["out_y"]
```
